# Optimizing a Trainium2 kernel written in Bass

```python
import numpy as np
import jax
import jax.numpy as jnp

def _softmax(x, axis=-1):
    return jax.nn.softmax(x, axis=axis)

def _gelu(x):
    return jax.nn.gelu(x, approximate=True)

def _silu(x):
    return jax.nn.silu(x)

def _sigmoid(x):
    return jax.nn.sigmoid(x)

def _layernorm(x, axis=-1, eps=1e-05):
    m = jnp.mean(x, axis=axis, keepdims=True)
    v = jnp.var(x, axis=axis, keepdims=True)
    return (x - m) / jnp.sqrt(v + eps)

def _scatter_add(tgt, idx, src, axis=0):
    return tgt.at[idx].add(src)

def _segment_sum(src, seg, n):
    return jax.ops.segment_sum(src, seg, n)
kernel_name = 'mk_adj_resnorm_d1_adj_r2_9a4e15'

def setup_inputs(seed: int=0):
    np.random.seed(seed)
    _w = jnp.asarray

    def _rec_inputs():
        import jax
        import jax.numpy as jnp
        _gk = jax.random.key(seed)
        x = 7.22e-05 + 1 * jax.random.normal(jax.random.fold_in(_gk, 1), (128, 128, 512), jnp.float32)
        _a = jax.random.bernoulli(jax.random.fold_in(_gk, 2), 0.03125, (128, 128, 128))
        _a = jnp.logical_or(_a, jnp.eye(128, dtype=bool))
        adj = _a.astype(jnp.int32)
        return (x, adj)
    x, adj = _rec_inputs()

    def _L0_gnn_setup():
        import jax, jax.numpy as jnp
        import numpy as np
        import math
        D_MODEL = 512
        N_HEADS = 16
        D_HEAD = D_MODEL // N_HEADS
        B, S = (4, 1024)
        key = jax.random.key(seed)
        ks = jax.random.split(key, 10)
        x = jax.random.normal(ks[0], (B, S, D_MODEL), dtype=jnp.float32)
        mask = jax.random.randint(ks[1], (B, S, S), 0, 2, dtype=jnp.int32)
        eye = jnp.eye(S, dtype=jnp.int32)[None]
        mask = jnp.maximum(mask, eye)
        std = 1.0 / math.sqrt(D_MODEL)
        Wq = jax.random.normal(ks[2], (D_MODEL, D_MODEL), dtype=jnp.float32) * std
        Wk = jax.random.normal(ks[3], (D_MODEL, D_MODEL), dtype=jnp.float32) * std
        Wv = jax.random.normal(ks[4], (D_MODEL, D_MODEL), dtype=jnp.float32) * std
        Wo = jax.random.normal(ks[5], (D_MODEL, D_MODEL), dtype=jnp.float32) * std
        bq = jnp.zeros((D_MODEL,), dtype=jnp.float32)
        bk = jnp.zeros((D_MODEL,), dtype=jnp.float32)
        bv = jnp.zeros((D_MODEL,), dtype=jnp.float32)
        bo = jnp.zeros((D_MODEL,), dtype=jnp.float32)
        return {'x': x, 'mask': mask, 'Wq': Wq, 'bq': bq, 'Wk': Wk, 'bk': bk, 'Wv': Wv, 'bv': bv, 'Wo': Wo, 'bo': bo}
    _L0_gnn_all = _L0_gnn_setup()
    _L0_gnn_in = {k: v for k, v in _L0_gnn_all.items() if k in ('Wq', 'bq', 'Wk', 'bk', 'Wv', 'bv', 'Wo', 'bo')}
    del _L0_gnn_all
    return {'x': x, 'adj': adj, 'L0_gnn_Wq': _L0_gnn_in['Wq'], 'L0_gnn_bq': _L0_gnn_in['bq'], 'L0_gnn_Wk': _L0_gnn_in['Wk'], 'L0_gnn_bk': _L0_gnn_in['bk'], 'L0_gnn_Wv': _L0_gnn_in['Wv'], 'L0_gnn_bv': _L0_gnn_in['bv'], 'L0_gnn_Wo': _L0_gnn_in['Wo'], 'L0_gnn_bo': _L0_gnn_in['bo']}

def reference(x, adj, L0_gnn_Wq, L0_gnn_bq, L0_gnn_Wk, L0_gnn_bk, L0_gnn_Wv, L0_gnn_bv, L0_gnn_Wo, L0_gnn_bo):
    import jax
    import jax.numpy as jnp

    def _L0_gnn_ref(x, mask, Wq, bq, Wk, bk, Wv, bv, Wo, bo):
        import jax, jax.numpy as jnp
        import numpy as np
        import math
        D_MODEL = 512
        N_HEADS = 16
        D_HEAD = D_MODEL // N_HEADS
        B, S = (4, 1024)
        b, s, _ = x.shape
        scale = 1.0 / math.sqrt(D_HEAD)

        def heads(t):
            return t.reshape(b, s, N_HEADS, D_HEAD).transpose(0, 2, 1, 3)
        q = heads(x @ Wq + bq)
        k = heads(x @ Wk + bk)
        v = heads(x @ Wv + bv)
        scores = jnp.einsum('bhqd,bhkd->bhqk', q, k) * scale
        scores = jnp.where(mask[:, None] == 0, -jnp.inf, scores)
        attn = jax.nn.softmax(scores, axis=-1)
        out = jnp.einsum('bhqk,bhkd->bhqd', attn, v)
        out = out.transpose(0, 2, 1, 3).reshape(b, s, D_MODEL)
        return out @ Wo + bo
    x = _layernorm(x + _L0_gnn_ref(x, adj, L0_gnn_Wq, L0_gnn_bq, L0_gnn_Wk, L0_gnn_bk, L0_gnn_Wv, L0_gnn_bv, L0_gnn_Wo, L0_gnn_bo), axis=-1)
    return x

_drawn_inputs = setup_inputs


def setup_inputs(seed=0):
    import zlib

    import numpy as np

    out = dict(_drawn_inputs(seed))
    spreads = {'L0_gnn_bq': (0.0, 0.1),
     'L0_gnn_bk': (0.0, 0.1),
     'L0_gnn_bv': (0.0, 0.1),
     'L0_gnn_bo': (0.0, 0.1)}
    factors = {}
    for name, (base, spread) in spreads.items():
        noise = np.random.default_rng([zlib.crc32(name.encode()), seed]).standard_normal(out[name].shape)
        drawn = base * np.exp(spread * noise) if base else spread * noise
        out[name] = jnp.asarray(drawn.astype(out[name].dtype))
    for name, factor in factors.items():
        out[name] = (out[name] * factor).astype(out[name].dtype)
    return out
```

```python
from contextlib import ExitStack

import concourse.bass as bass
from concourse import mybir

ALU = mybir.AluOpType
ACT = mybir.ActivationFunctionType
F32 = mybir.dt.float32
F32R = mybir.dt.float32r
I32 = mybir.dt.int32
AX_X = mybir.AxisListType.X

P = 128
GB = 4
ROUND = 8
DH = 32
MASKED = -3.0e38
EPS = 1e-5


def gnn_attention(nc, x, adj, Wq, bq, Wk, bk, Wv, bv, Wo, bo, out):
    NB, S, D = x.shape
    KC = D // P
    H = D // DH
    HC = H // KC
    TOK = GB * S
    SCALE = float(DH) ** -0.5
    assert S == P and KC == GB == HC == 4 and NB % ROUND == 0

    FIRST, LAST = -ROUND, NB + 1
    BODY = 3
    ROUNDS = (NB - ROUND - BODY) // ROUND
    TAIL = BODY + ROUND * ROUNDS

    with ExitStack() as ctx:

        def sb(name, shape, dt=F32):
            return ctx.enter_context(nc.sbuf_tensor(name, shape, dt))

        def bank(name, shape):
            return ctx.enter_context(nc.psum_tensor(name, shape, F32))

        def sem(name):
            return ctx.enter_context(nc.semaphore(name))

        w_hi = [sb(f"w{w}_hi", [P, KC, D], F32R) for w in "qkvo"]
        w_lo = [sb(f"w{w}_lo", [P, KC, D], F32R) for w in "qkvo"]
        x_in = [sb(f"x_in{i}", [P, GB, D]) for i in range(2)]
        xT_hi = [sb(f"xT_hi{i}", [P, KC, TOK], F32R) for i in range(2)]
        xT_lo = [sb(f"xT_lo{i}", [P, KC, TOK], F32R) for i in range(2)]
        qT = [sb(f"qT{i}", [P, KC, TOK]) for i in range(2)]
        kT = [sb(f"kT{i}", [P, KC, TOK]) for i in range(2)]
        v = sb("v", [P, ROUND, D])
        probs = [sb(f"probs{i}", [P, H, S]) for i in range(2)]
        probsT = sb("probsT", [P, H, S])
        oT_hi = sb("oT_hi", [P, KC, S], F32R)
        oT_lo = sb("oT_lo", [P, KC, S], F32R)
        rows = sb("rows", [P, 4, D])
        adj_in = [sb(f"adj_in{i}", [P, GB, S], I32) for i in range(2)]
        mask_add = sb("mask_add", [P, 2, S])
        ident = sb("ident", [P, P])
        bq_col = sb("bq_col", [P, KC])
        bq_scaled = sb("bq_scaled", [P, KC])
        bk_col = sb("bk_col", [P, KC])
        bv_all = sb("bv_all", [P, D])
        bo_all = sb("bo_all", [P, D])
        neg_max = sb("neg_max", [P, 2, H])
        exp_sum = sb("exp_sum", [P, 2, H])
        inv_sum = sb("inv_sum", [P, 2, H])
        moments = sb("moments", [P, 2, 6])
        mean_var = sb("mean_var", [P, 2, 2])
        var_eps = sb("var_eps", [P, 2])
        rstd = sb("rstd", [P, 2])
        minus_half = sb("minus_half", [P, 1])
        eps = sb("eps", [P, 1])

        scores = bank("scores", [P, HC, KC * S])
        pT_bank = [bank(f"pT_bank{i}", [P, HC * S]) for i in range(2)]
        bank_a = bank("bank_a", [P, D])
        bank_b = bank("bank_b", [P, D])

        w_loaded = [sem(f"w{w}_loaded") for w in "qkvo"]
        consts_loaded = sem("consts_loaded")
        x_loaded = [sem(f"x_loaded{i}") for i in range(2)]
        adj_loaded = [sem(f"adj_loaded{i}") for i in range(2)]
        rows_loaded = [sem(f"rows_loaded{i}") for i in range(4)]
        rows_stored = [sem(f"rows_stored{i}") for i in range(4)]
        cleared = sem("cleared")
        ident_ready = sem("ident_ready")
        w_hi_ready = sem("w_hi_ready")
        w_lo_ready = sem("w_lo_ready")
        bq_ready = sem("bq_ready")
        xT_done, xT_hi_ready, xT_lo_ready = sem("xT_done"), sem("xT_hi_ready"), sem("xT_lo_ready")
        q_done, q_ready = sem("q_done"), sem("q_ready")
        k_done, k_ready = sem("k_done"), sem("k_ready")
        v_done, v_ready = sem("v_done"), sem("v_ready")
        scores_done, masked, mask_ready = sem("scores_done"), sem("masked"), sem("mask_ready")
        o_done, o_hi_ready, o_lo_ready = sem("o_done"), sem("o_hi_ready"), sem("o_lo_ready")
        y_done, y_added, bo_added = sem("y_done"), sem("y_added"), sem("bo_added")
        moments_ready, mean_ready = sem("moments_ready"), sem("mean_ready")
        var_ready, rstd_ready, normed = sem("var_ready"), sem("rstd_ready"), sem("normed")
        max_ready, exp_ready = sem("max_ready"), sem("exp_ready")
        inv_ready, probs_ready = sem("inv_ready"), sem("probs_ready")
        pT_done, pT_ready = sem("pT_done"), sem("pT_ready")

        class Step:

            def __init__(self, n, u):
                self.n, self.u = n, u
                self.peeled = isinstance(n, int)

            def has(self, ahead):
                return not self.peeled or 0 <= ROUND * self.n + self.u + ahead < NB

            def slot(self, ahead, slots):
                return (self.u + ahead) % slots

            def group(self, ahead):
                return (self.u + ahead) // GB % 2

            def fills(self, ahead, slots):
                return (ROUND // slots) * self.n + (self.u + ahead) // slots + 1

            def batch(self, ahead):
                return ROUND * self.n + (self.u + ahead)

        def wait(eng, semaphore, step, ahead, per=1, more=0):
            if step.peeled:
                upto = per * step.batch(ahead) + (more if per > 1 else 1)
                upto = min(upto, per * NB)
                if upto > 0:
                    eng.wait_ge(semaphore, upto)
            else:
                eng.wait_ge(semaphore, per * ROUND * step.n + (per * (step.u + ahead) + (more if per > 1 else 1)))

        def run(eng, do_step):
            for s in range(FIRST, BODY):
                do_step(Step(s // ROUND, s % ROUND))
            with eng.Fori(0, ROUNDS) as n:
                for u in range(BODY, BODY + ROUND):
                    do_step(Step(n, u))
            for s in range(TAIL, LAST + 1):
                do_step(Step(s // ROUND, s % ROUND))

        block = ctx.enter_context(nc.Block())

        @block.sync
        def _(sp):
            staging = [probs[0], probs[1], probsT, rows]
            sp.dma_start(x_in[0][:], x[0:GB].rearrange("b t d -> t b d")).then_inc(x_loaded[0], 16)
            for w, dram in enumerate((Wq, Wk, Wv, Wo)):
                flat = staging[w][:].rearrange("p a b -> p (a b)").rearrange("p (c n) -> p c n", c=KC)
                sp.dma_start(flat, dram.rearrange("(c p) n -> p c n", p=P)).then_inc(w_loaded[w], 16)
            sp.dma_start(bq_col[:], bq.rearrange("(c p) -> p c", p=P),
                         allow_slow_non_contiguous=True).then_inc(consts_loaded, 16)
            sp.dma_start(bk_col[:], bk.rearrange("(c p) -> p c", p=P),
                         allow_slow_non_contiguous=True).then_inc(consts_loaded, 16)
            sp.dma_start(bv_all[:], bv.partition_broadcast(P)).then_inc(consts_loaded, 16)
            sp.dma_start(bo_all[:], bo.partition_broadcast(P)).then_inc(consts_loaded, 16)

            def step(st):
                u = st.u
                if st.has(-3):
                    slot = st.slot(-3, 4)
                    wait(sp, normed, st, -3)
                    sp.dma_start(out[bass.ds(st.batch(-3), 1)].rearrange("b t d -> t (b d)"),
                                 rows[:, slot, :]).then_inc(rows_stored[slot], 16)
                if st.has(0):
                    slot = st.slot(0, 4)
                    if not st.peeled or st.batch(0) >= 4:
                        sp.wait_ge(rows_stored[slot], 16 * (st.fills(0, 4) - 1))
                    else:
                        sp.wait_ge(w_lo_ready, 4)
                    sp.dma_start(rows[:, slot, :],
                                 x[bass.ds(st.batch(0), 1)].rearrange("b t d -> t (b d)")
                                 ).then_inc(rows_loaded[slot], 16)
                if u % GB == 0 and st.has(12):
                    g = st.group(12)
                    wait(sp, xT_done, st, 7)
                    sp.dma_start(x_in[g][:], x[bass.ds(st.batch(12), GB)].rearrange("b t d -> t b d")
                                 ).then_inc(x_loaded[g], 16)
                if u % GB == 0 and st.has(4):
                    g = st.group(4)
                    wait(sp, mask_ready, st, -1)
                    sp.dma_start(adj_in[g][:], adj[bass.ds(st.batch(4), GB)].rearrange("b q k -> q b k")
                                 ).then_inc(adj_loaded[g], 16)

            run(sp, step)
            for slot in range(4):
                b = NB - 4 + slot
                if b == NB - 1:
                    sp.wait_ge(normed, NB)
                    sp.dma_start(out[b:b + 1].rearrange("b t d -> t (b d)"),
                                 rows[:, slot, :]).then_inc(rows_stored[slot], 16)
            for slot in range(4):
                sp.wait_ge(rows_stored[slot], 16 * (NB // 4))

        @block.gpsimd
        def _(pool):
            nc.gpsimd.memset(ident[:], 0.0).then_inc(cleared, 1)
            nc.gpsimd.memset(minus_half[:], -0.5).then_inc(cleared, 1)
            nc.gpsimd.memset(eps[:], EPS).then_inc(cleared, 1)
            pool.wait_ge(cleared, 3)
            nc.gpsimd.affine_select(out=ident[:], in_=ident[:], compare_op=ALU.not_equal, fill=1.0, base=0,
                                    pattern=[[-1, P]], channel_multiplier=1).then_inc(ident_ready, 1)
            pool.wait_ge(consts_loaded, 64)

            def step(st):
                if st.has(1):
                    if st.u % GB == GB - 1:
                        pool.wait_ge(adj_loaded[st.group(1)], 16 * st.fills(1, ROUND))
                    wait(pool, masked, st, -1)
                if st.has(-1):
                    slot = st.slot(-1, 4)
                    pool.wait_ge(rows_loaded[slot], 16 * st.fills(-1, 4))
                    nc.gpsimd.tensor_tensor(rows[:, slot, :], rows[:, slot, :], bo_all[:],
                                            ALU.add).then_inc(bo_added, 1)
                if st.has(1):
                    nc.gpsimd.tensor_scalar(mask_add[:, st.slot(1, 2), :],
                                            adj_in[st.group(1)][:, st.slot(1, GB), :],
                                            0.0, MASKED, ALU.is_equal, ALU.mult).then_inc(mask_ready, 1)
                if st.has(-2):
                    two = st.slot(-2, 2)
                    wait(pool, mean_ready, st, -2)
                    nc.gpsimd.tensor_tensor(var_eps[:, two:two + 1], mean_var[:, two, 1:2], eps[:],
                                            ALU.add).then_inc(var_ready, 1)
                    wait(pool, var_ready, st, -2)
                    nc.gpsimd.tensor_tensor(rstd[:, two:two + 1], var_eps[:, two:two + 1], minus_half[:],
                                            ALU.pow).then_inc(rstd_ready, 1)

            run(pool, step)

        @block.scalar
        def _(act):
            staging = [probs[0], probs[1], probsT, rows]
            for w in range(4):
                act.wait_ge(w_loaded[w], 16)
                nc.scalar.activation(w_hi[w][:].rearrange("p c n -> p (c n)"),
                                     staging[w][:].rearrange("p a b -> p (a b)"),
                                     ACT.Copy).then_inc(w_hi_ready, 1)
            act.wait_ge(bq_ready, 1)

            def exps(st, c):
                two = st.slot(0, 2)
                wait(act, max_ready, st, 0, per=4, more=c + 1)
                for h in range(HC * c, HC * (c + 1)):
                    last = nc.scalar.activation(probs[two][:, h, :], probs[two][:, h, :], ACT.Exp,
                                                bias=neg_max[:, two, h:h + 1],
                                                accum_out=exp_sum[:, two, h:h + 1])
                last.then_inc(exp_ready, 1)

            def probsT_out(st, c):
                wait(act, pT_done, st, -1, per=4, more=c + 1)
                nc.scalar.activation(probsT[:, HC * c:HC * (c + 1), :].rearrange("p h q -> p (h q)"),
                                     pT_bank[c % 2][:], ACT.Copy).then_inc(pT_ready, 1)

            def step(st):
                chunk = st.u % GB
                if st.has(-2):
                    wait(act, o_done, st, -2)
                    nc.scalar.activation(oT_hi[:].rearrange("p c q -> p (c q)"), bank_a[:],
                                         ACT.Copy).then_inc(o_hi_ready, 1)
                if st.has(8):
                    wait(act, xT_done, st, 8)
                    nc.scalar.activation(xT_hi[st.group(8)][:, chunk, :], bank_a[:],
                                         ACT.Copy).then_inc(xT_hi_ready, 1)
                if st.has(0):
                    exps(st, 0)
                if st.has(4):
                    wait(act, q_done, st, 4)
                    nc.scalar.activation(qT[st.group(4)][:, chunk, :], bank_b[:], ACT.Identity,
                                         bias=bq_scaled[:, chunk:chunk + 1], scale=SCALE).then_inc(q_ready, 1)
                if st.has(0):
                    exps(st, 1)
                if st.has(-1):
                    probsT_out(st, 0)
                    probsT_out(st, 1)
                if st.has(0):
                    exps(st, 2)
                if st.has(4):
                    wait(act, k_done, st, 4)
                    nc.scalar.activation(kT[st.group(4)][:, chunk, :], bank_a[:], ACT.Identity,
                                         bias=bk_col[:, chunk:chunk + 1]).then_inc(k_ready, 1)
                if st.has(-1):
                    probsT_out(st, 2)
                    probsT_out(st, 3)
                if st.has(0):
                    exps(st, 3)

            run(act, step)

        @block.vector
        def _(dve):
            staging = [probs[0], probs[1], probsT, rows]
            dve.wait_ge(consts_loaded, 64)
            nc.vector.tensor_scalar(bq_scaled[:], bq_col[:], SCALE, None, ALU.mult).then_inc(bq_ready, 1)
            for w in range(4):
                dve.wait_ge(w_hi_ready, w + 1)
                nc.vector.tensor_tensor(w_lo[w][:].rearrange("p c n -> p (c n)"),
                                        staging[w][:].rearrange("p a b -> p (a b)"),
                                        w_hi[w][:].bitcast(F32).rearrange("p c n -> p (c n)"),
                                        ALU.subtract).then_inc(w_lo_ready, 1)

            def maxima(st, c):
                two = st.slot(0, 2)
                nc.vector.tensor_reduce(neg_max[:, two, HC * c:HC * (c + 1)],
                                        probs[two][:, HC * c:HC * (c + 1), :], axis=AX_X, op=ALU.max,
                                        negate=True).then_inc(max_ready, 1)

            def inverses(st, c):
                two = st.slot(0, 2)
                wait(dve, exp_ready, st, 0, per=4, more=c + 1)
                nc.vector.reciprocal(inv_sum[:, two, HC * c:HC * (c + 1)],
                                     exp_sum[:, two, HC * c:HC * (c + 1)]).then_inc(inv_ready, 1)

            def normalise(st, ahead, c):
                two = st.slot(ahead, 2)
                heads = slice(HC * c, HC * (c + 1))
                wait(dve, inv_ready, st, ahead, per=4, more=c + 1)
                nc.vector.tensor_tensor(probs[two][:, heads, :], probs[two][:, heads, :],
                                        inv_sum[:, two, heads].unsqueeze(2).broadcast_to([P, HC, S]),
                                        ALU.mult).then_inc(probs_ready, 1)

            def step(st):
                chunk, two = st.u % GB, st.slot(0, 2)
                if st.has(-2):
                    wait(dve, o_hi_ready, st, -2)
                    nc.vector.tensor_tensor(oT_lo[:].rearrange("p c q -> p (c q)"), bank_a[:],
                                            oT_hi[:].bitcast(F32).rearrange("p c q -> p (c q)"),
                                            ALU.subtract).then_inc(o_lo_ready, 1)
                if st.has(0):
                    wait(dve, scores_done, st, 0)
                    wait(dve, mask_ready, st, 0)
                    nc.vector.tensor_tensor(
                        probs[two][:].rearrange("p (c j) k -> p j c k", j=HC),
                        scores[:].rearrange("p j (c k) -> p j c k", c=KC),
                        mask_add[:, two, :].unsqueeze(1).unsqueeze(1).broadcast_to([P, HC, KC, S]),
                        ALU.add).then_inc(masked, 1)
                if st.has(-2):
                    slot, half = st.slot(-2, 4), st.slot(-2, 2)
                    wait(dve, y_done, st, -2)
                    wait(dve, bo_added, st, -2)
                    nc.vector.tensor_tensor(rows[:, slot, :], bank_b[:], rows[:, slot, :],
                                            ALU.add).then_inc(y_added, 1)
                if st.has(0):
                    wait(dve, masked, st, 0)
                    maxima(st, 0)
                if st.has(-2):
                    wait(dve, y_added, st, -2)
                    nc.vector.bn_stats(moments[:, half, :], rows[:, slot, :]).then_inc(moments_ready, 1)
                if st.has(8):
                    wait(dve, xT_hi_ready, st, 8)
                    nc.vector.tensor_tensor(xT_lo[st.group(8)][:, chunk, :], bank_a[:],
                                            xT_hi[st.group(8)][:, chunk, :].bitcast(F32),
                                            ALU.subtract).then_inc(xT_lo_ready, 1)
                if st.has(-2):
                    wait(dve, moments_ready, st, -2)
                if st.has(0):
                    maxima(st, 1)
                if st.has(-2):
                    nc.vector.bn_aggr(mean_var[:, half, :], moments[:, half, :]).then_inc(mean_ready, 1)
                if st.has(0):
                    maxima(st, 2)
                    maxima(st, 3)
                    inverses(st, 0)
                if st.has(-2):
                    wait(dve, rstd_ready, st, -2)
                    nc.vector.tensor_scalar(rows[:, slot, :], rows[:, slot, :], mean_var[:, half, 0:1],
                                            rstd[:, half:half + 1], ALU.subtract, ALU.mult).then_inc(normed, 1)
                if st.has(0):
                    inverses(st, 1)
                    normalise(st, 0, 0)
                    normalise(st, 0, 1)
                    inverses(st, 2)
                if st.has(4):
                    wait(dve, v_done, st, 4)
                    nc.vector.tensor_tensor(v[:, st.slot(4, ROUND), :], bank_b[:], bv_all[:],
                                            ALU.add).then_inc(v_ready, 1)
                if st.has(0):
                    inverses(st, 3)
                    normalise(st, 0, 2)
                    normalise(st, 0, 3)

            run(dve, step)

        @block.tensor
        def _(pe):
            pe.wait_ge(ident_ready, 1)

            def three_passes(dst, left, right):
                for c in range(KC):
                    for a, b in ((0, 0), (0, 1), (1, 0)):
                        last = nc.tensor.matmul(dst, left[a](c), right[b](c), start=(c == 0 and a == b),
                                                stop=(c == KC - 1 and a == 1))
                return last

            def probs_transposed(st, c):
                two = st.slot(-1, 2)
                wait(pe, probs_ready, st, -1, per=4, more=c + 1)
                wait(pe, pT_ready, st, -1, per=4, more=c - 1)
                for j in range(HC):
                    last = nc.tensor.transpose(pT_bank[c % 2][:, j * S:(j + 1) * S],
                                               probs[two][:, HC * c + j, :], ident[:])
                last.then_inc(pT_done, 1)

            def step(st):
                chunk = st.u % GB
                cols = slice(chunk * P, (chunk + 1) * P)
                g = st.group(4)
                if st.has(0):
                    if chunk == 0:
                        wait(pe, q_ready, st, 3)
                        wait(pe, k_ready, st, 3)
                    wait(pe, masked, st, -1)
                    for c in range(KC):
                        for j in range(HC):
                            rows_j = slice(DH * j, DH * (j + 1))
                            last = nc.tensor.matmul(scores[:, j, c * S:(c + 1) * S],
                                                    qT[st.group(0)][rows_j, c, cols],
                                                    kT[st.group(0)][rows_j, c, cols],
                                                    start=True, stop=True, tile_position=(DH * j, 0))
                    last.then_inc(scores_done, 1)
                if st.has(-2):
                    if st.peeled and st.batch(-2) == 0:
                        pe.wait_ge(w_lo_ready, 4)
                    wait(pe, o_lo_ready, st, -2)
                    wait(pe, v_ready, st, 3)
                    wait(pe, y_added, st, -3)
                    three_passes(bank_b[:], [lambda c: oT_hi[:, c, :], lambda c: oT_lo[:, c, :]],
                                 [lambda c: w_hi[3][:, c, :], lambda c: w_lo[3][:, c, :]]).then_inc(y_done, 1)
                if st.has(8):
                    if chunk == 0:
                        pe.wait_ge(x_loaded[st.group(8)], 16 * st.fills(8, ROUND))
                    if st.has(-2):
                        wait(pe, o_lo_ready, st, -2)
                    else:
                        wait(pe, k_ready, st, 3)
                        wait(pe, xT_lo_ready, st, 7)
                    for b in range(GB):
                        last = nc.tensor.transpose(bank_a[:, b * S:(b + 1) * S],
                                                   x_in[st.group(8)][:, b, cols], ident[:])
                    last.then_inc(xT_done, 1)
                if st.has(4):
                    if chunk == 0:
                        wait(pe, xT_lo_ready, st, 7)
                    if st.peeled and st.batch(4) == 0:
                        pe.wait_ge(w_lo_ready, 3)
                    wait(pe, y_added, st, -2)
                    wait(pe, v_ready, st, 3)
                    three_passes(bank_b[:], [lambda c: w_hi[0][:, c, cols], lambda c: w_lo[0][:, c, cols]],
                                 [lambda c: xT_hi[g][:, c, :], lambda c: xT_lo[g][:, c, :]]).then_inc(q_done, 1)
                if st.has(-1):
                    probs_transposed(st, 0)
                    probs_transposed(st, 1)
                if st.has(4):
                    wait(pe, xT_lo_ready, st, 8)
                    three_passes(bank_a[:], [lambda c: w_hi[1][:, c, cols], lambda c: w_lo[1][:, c, cols]],
                                 [lambda c: xT_hi[g][:, c, :], lambda c: xT_lo[g][:, c, :]]).then_inc(k_done, 1)
                if st.has(-1):
                    probs_transposed(st, 2)
                    probs_transposed(st, 3)
                if st.has(4):
                    wait(pe, q_ready, st, 4)
                    three_passes(bank_b[:], [lambda c: xT_hi[g][:, c, cols], lambda c: xT_lo[g][:, c, cols]],
                                 [lambda c: w_hi[2][:, c, :], lambda c: w_lo[2][:, c, :]]).then_inc(v_done, 1)
                if st.has(-1):
                    wait(pe, k_ready, st, 4)
                    wait(pe, v_ready, st, -1)
                    for c in range(KC):
                        wait(pe, pT_ready, st, -1, per=4, more=c + 1)
                        for j in range(HC):
                            h = HC * c + j
                            last = nc.tensor.matmul(bank_a[DH * j:DH * (j + 1), c * S:(c + 1) * S],
                                                    v[:, st.slot(-1, ROUND), DH * h:DH * (h + 1)],
                                                    probsT[:, h, :], start=True, stop=True,
                                                    tile_position=(0, DH * j))
                    last.then_inc(o_done, 1)

            run(pe, step)


_INS = ['x', 'adj', 'L0_gnn_Wq', 'L0_gnn_bq', 'L0_gnn_Wk', 'L0_gnn_bk', 'L0_gnn_Wv', 'L0_gnn_bv',
        'L0_gnn_Wo', 'L0_gnn_bo']


def kernel(**inputs):
    import numpy as _np
    import concourse.bacc as _bacc
    from concourse import mybir as _mybir
    from concourse.bass_utils import run_bass_kernel_spmd as _run

    nc = _bacc.Bacc("TRN2", target_bir_lowering=False, num_devices=1)
    arrays, args = {}, []
    for name in _INS:
        a = _np.ascontiguousarray(inputs[name])
        arrays[f"in_{name}_dram"] = a
        args.append(nc.dram_tensor(f"in_{name}_dram", a.shape, _mybir.dt.from_np(a.dtype), kind="ExternalInput").ap())
    shape = arrays["in_x_dram"].shape
    args.append(nc.dram_tensor("out_dram", shape, _mybir.dt.float32, kind="ExternalOutput").ap())
    gnn_attention(nc, *args)
    r = _run(nc, [arrays], core_ids=[0])
    return r.results[0]["out_dram"]
```

```python
from contextlib import ExitStack

import concourse.bass as bass
from concourse import mybir

ALU = mybir.AluOpType
ACT = mybir.ActivationFunctionType
F32 = mybir.dt.float32
F32R = mybir.dt.float32r
I32 = mybir.dt.int32
AX_X = mybir.AxisListType.X

P = 128
GB = 4
ROUND = 8
DH = 32
MASKED = -3.0e38
EPS = 1e-5


def gnn_attention(nc, x, adj, Wq, bq, Wk, bk, Wv, bv, Wo, bo, out):
    NB, S, D = x.shape
    KC = D // P
    H = D // DH
    HC = H // KC
    TOK = GB * S
    SCALE = float(DH) ** -0.5
    assert S == P and KC == GB == HC == 4 and NB % ROUND == 0

    FIRST, LAST = -ROUND, NB + 1
    BODY = 3
    ROUNDS = (NB - ROUND - BODY) // ROUND
    TAIL = BODY + ROUND * ROUNDS

    with ExitStack() as ctx:

        def sb(name, shape, dt=F32):
            return ctx.enter_context(nc.sbuf_tensor(name, shape, dt))

        def bank(name, shape):
            return ctx.enter_context(nc.psum_tensor(name, shape, F32))

        def sem(name):
            return ctx.enter_context(nc.semaphore(name))

        w_hi = [sb(f"w{w}_hi", [P, KC, D], F32R) for w in "qkvo"]
        w_lo = [sb(f"w{w}_lo", [P, KC, D], F32R) for w in "qkvo"]
        x_in = sb("x_in", [P, KC, TOK])
        xT_raw = sb("xT_raw", [P, TOK])
        xT_hi = [sb(f"xT_hi{i}", [P, KC, TOK], F32R) for i in range(2)]
        xT_lo = [sb(f"xT_lo{i}", [P, KC, TOK], F32R) for i in range(2)]
        qT = [sb(f"qT{i}", [P, KC, TOK]) for i in range(2)]
        kT = [sb(f"kT{i}", [P, KC, TOK]) for i in range(2)]
        v = sb("v", [P, ROUND, D])
        probs = [sb(f"probs{i}", [P, H, S]) for i in range(2)]
        probsT = sb("probsT", [P, H, S])
        oT_hi = sb("oT_hi", [P, KC, S], F32R)
        oT_lo = sb("oT_lo", [P, KC, S], F32R)
        rows = sb("rows", [P, 4, D])
        adj_in = [sb(f"adj_in{i}", [P, GB, S], I32) for i in range(2)]
        mask_add = sb("mask_add", [P, 2, S])
        ident = sb("ident", [P, P])
        bq_col = sb("bq_col", [P, KC])
        bq_scaled = sb("bq_scaled", [P, KC])
        bk_col = sb("bk_col", [P, KC])
        bv_all = sb("bv_all", [P, D])
        bo_all = sb("bo_all", [P, D])
        neg_max = sb("neg_max", [P, 2, H])
        exp_sum = sb("exp_sum", [P, 2, H])
        inv_sum = sb("inv_sum", [P, 2, H])
        moments = sb("moments", [P, 2, 6])
        mean_var = sb("mean_var", [P, 2, 2])
        var_eps = sb("var_eps", [P, 2])
        rstd = sb("rstd", [P, 2])
        minus_half = sb("minus_half", [P, 1])
        eps = sb("eps", [P, 1])

        scores = bank("scores", [P, HC, KC * S])
        pT_bank = [bank(f"pT_bank{i}", [P, HC * S]) for i in range(2)]
        bank_a = bank("bank_a", [P, D])
        bank_b = bank("bank_b", [P, D])

        w_loaded = [sem(f"w{w}_loaded") for w in "qkvo"]
        consts_loaded = sem("consts_loaded")
        x_loaded = [sem(f"x_loaded{i}") for i in range(KC)]
        adj_loaded = [sem(f"adj_loaded{i}") for i in range(2)]
        rows_loaded = [sem(f"rows_loaded{i}") for i in range(4)]
        rows_stored = [sem(f"rows_stored{i}") for i in range(4)]
        cleared = sem("cleared")
        ident_ready = sem("ident_ready")
        w_hi_ready = sem("w_hi_ready")
        w_lo_ready = sem("w_lo_ready")
        bq_ready = sem("bq_ready")
        xT_done, xT_hi_ready, xT_lo_ready = sem("xT_done"), sem("xT_hi_ready"), sem("xT_lo_ready")
        q_done, q_ready = sem("q_done"), sem("q_ready")
        k_done, k_ready = sem("k_done"), sem("k_ready")
        v_done, v_ready = sem("v_done"), sem("v_ready")
        scores_done, masked, mask_ready = sem("scores_done"), sem("masked"), sem("mask_ready")
        o_done, o_hi_ready, o_lo_ready = sem("o_done"), sem("o_hi_ready"), sem("o_lo_ready")
        y_done, y_added, bo_added = sem("y_done"), sem("y_added"), sem("bo_added")
        moments_ready, mean_ready = sem("moments_ready"), sem("mean_ready")
        var_ready, rstd_ready, normed = sem("var_ready"), sem("rstd_ready"), sem("normed")
        max_ready, exp_ready = sem("max_ready"), sem("exp_ready")
        inv_ready, probs_ready = sem("inv_ready"), sem("probs_ready")
        pT_done, pT_ready = sem("pT_done"), sem("pT_ready")

        class Step:

            def __init__(self, n, u):
                self.n, self.u = n, u
                self.peeled = isinstance(n, int)

            def has(self, ahead):
                return not self.peeled or 0 <= ROUND * self.n + self.u + ahead < NB

            def slot(self, ahead, slots):
                return (self.u + ahead) % slots

            def group(self, ahead):
                return (self.u + ahead) // GB % 2

            def fills(self, ahead, slots):
                return (ROUND // slots) * self.n + (self.u + ahead) // slots + 1

            def batch(self, ahead):
                return ROUND * self.n + (self.u + ahead)

        def wait(eng, semaphore, step, ahead, per=1, more=0):
            if step.peeled:
                upto = per * step.batch(ahead) + (more if per > 1 else 1)
                upto = min(upto, per * NB)
                if upto > 0:
                    eng.wait_ge(semaphore, upto)
            else:
                eng.wait_ge(semaphore, per * ROUND * step.n + (per * (step.u + ahead) + (more if per > 1 else 1)))

        def run(eng, do_step):
            for s in range(FIRST, BODY):
                do_step(Step(s // ROUND, s % ROUND))
            with eng.Fori(0, ROUNDS) as n:
                for u in range(BODY, BODY + ROUND):
                    do_step(Step(n, u))
            for s in range(TAIL, LAST + 1):
                do_step(Step(s // ROUND, s % ROUND))

        block = ctx.enter_context(nc.Block())

        @block.sync
        def _(sp):
            staging = [probs[0], probs[1], probsT, rows]

            def load_x(batch, c):
                blocks = x[bass.ds(batch, GB)].rearrange("b (k t) (c q f) -> c q t (b k) f", t=DH, q=HC, f=DH)
                for q in range(HC):
                    sp.dma_start(x_in[DH * q:DH * (q + 1), c, :].rearrange("t (b f) -> t b f", f=DH),
                                 blocks[c, q]).then_inc(x_loaded[c], 16)

            for c in range(KC):
                load_x(0, c)
            sp.dma_start(bq_col[:], bq.rearrange("(c p) -> p c", p=P),
                         allow_slow_non_contiguous=True).then_inc(consts_loaded, 16)
            sp.dma_start(bk_col[:], bk.rearrange("(c p) -> p c", p=P),
                         allow_slow_non_contiguous=True).then_inc(consts_loaded, 16)
            sp.dma_start(bv_all[:], bv.partition_broadcast(P)).then_inc(consts_loaded, 16)
            sp.dma_start(bo_all[:], bo.partition_broadcast(P)).then_inc(consts_loaded, 16)

            def load_weight(w, dram):
                flat = staging[w][:].rearrange("p a b -> p (a b)").rearrange("p (c n) -> p c n", c=KC)
                sp.dma_start(flat, dram.rearrange("(c p) n -> p c n", p=P)).then_inc(w_loaded[w], 16)

            load_weight(0, Wq)

            def step(st):
                u = st.u
                if st.has(-3):
                    slot = st.slot(-3, 4)
                    wait(sp, normed, st, -3)
                    sp.dma_start(out[bass.ds(st.batch(-3), 1)].rearrange("b t d -> t (b d)"),
                                 rows[:, slot, :]).then_inc(rows_stored[slot], 16)
                if st.has(0):
                    slot = st.slot(0, 4)
                    if not st.peeled or st.batch(0) >= 4:
                        sp.wait_ge(rows_stored[slot], 16 * (st.fills(0, 4) - 1))
                    else:
                        sp.wait_ge(w_lo_ready, 4)
                    sp.dma_start(rows[:, slot, :],
                                 x[bass.ds(st.batch(0), 1)].rearrange("b t d -> t (b d)")
                                 ).then_inc(rows_loaded[slot], 16)
                if st.has(12 - u % GB):
                    wait(sp, xT_done, st, 8)
                    load_x(st.batch(12 - u % GB), u % GB)
                if st.peeled and st.batch(0) == FIRST:
                    for w, dram in ((1, Wk), (2, Wv), (3, Wo)):
                        load_weight(w, dram)
                if u % GB == 0 and st.has(4):
                    g = st.group(4)
                    wait(sp, mask_ready, st, -1)
                    sp.dma_start(adj_in[g][:], adj[bass.ds(st.batch(4), GB)].rearrange("b q k -> q b k")
                                 ).then_inc(adj_loaded[g], 16)

            run(sp, step)
            for slot in range(4):
                b = NB - 4 + slot
                if b == NB - 1:
                    sp.wait_ge(normed, NB)
                    sp.dma_start(out[b:b + 1].rearrange("b t d -> t (b d)"),
                                 rows[:, slot, :]).then_inc(rows_stored[slot], 16)
            for slot in range(4):
                sp.wait_ge(rows_stored[slot], 16 * (NB // 4))

        @block.gpsimd
        def _(pool):
            nc.gpsimd.memset(ident[:], 0.0).then_inc(cleared, 1)
            nc.gpsimd.memset(minus_half[:], -0.5).then_inc(cleared, 1)
            nc.gpsimd.memset(eps[:], EPS).then_inc(cleared, 1)
            pool.wait_ge(cleared, 3)
            nc.gpsimd.affine_select(out=ident[:], in_=ident[:], compare_op=ALU.not_equal, fill=1.0, base=0,
                                    pattern=[[-1, P]], channel_multiplier=1).then_inc(ident_ready, 1)
            pool.wait_ge(consts_loaded, 64)

            def step(st):
                if st.has(1):
                    if st.u % GB == GB - 1:
                        pool.wait_ge(adj_loaded[st.group(1)], 16 * st.fills(1, ROUND))
                    wait(pool, masked, st, -1)
                if st.has(-1):
                    slot = st.slot(-1, 4)
                    pool.wait_ge(rows_loaded[slot], 16 * st.fills(-1, 4))
                    nc.gpsimd.tensor_tensor(rows[:, slot, :], rows[:, slot, :], bo_all[:],
                                            ALU.add).then_inc(bo_added, 1)
                if st.has(1):
                    nc.gpsimd.tensor_scalar(mask_add[:, st.slot(1, 2), :],
                                            adj_in[st.group(1)][:, st.slot(1, GB), :],
                                            0.0, MASKED, ALU.is_equal, ALU.mult).then_inc(mask_ready, 1)
                if st.has(-2):
                    two = st.slot(-2, 2)
                    wait(pool, mean_ready, st, -2)
                    nc.gpsimd.tensor_tensor(var_eps[:, two:two + 1], mean_var[:, two, 1:2], eps[:],
                                            ALU.add).then_inc(var_ready, 1)
                    wait(pool, var_ready, st, -2)
                    nc.gpsimd.tensor_tensor(rstd[:, two:two + 1], var_eps[:, two:two + 1], minus_half[:],
                                            ALU.pow).then_inc(rstd_ready, 1)

            run(pool, step)

        @block.scalar
        def _(act):
            staging = [probs[0], probs[1], probsT, rows]

            def weight_hi(w):
                act.wait_ge(w_loaded[w], 16)
                nc.scalar.activation(w_hi[w][:].rearrange("p c n -> p (c n)"),
                                     staging[w][:].rearrange("p a b -> p (a b)"),
                                     ACT.Copy).then_inc(w_hi_ready, 1)
                if w == 0:
                    act.wait_ge(bq_ready, 1)

            def exps(st, ahead, c):
                two = st.slot(ahead, 2)
                wait(act, max_ready, st, ahead, per=4, more=c + 1)
                for h in range(HC * c, HC * (c + 1)):
                    last = nc.scalar.activation(probs[two][:, h, :], probs[two][:, h, :], ACT.Exp,
                                                bias=neg_max[:, two, h:h + 1],
                                                accum_out=exp_sum[:, two, h:h + 1])
                last.then_inc(exp_ready, 1)

            def probsT_out(st, c):
                wait(act, pT_done, st, -1, per=4, more=c + 1)
                nc.scalar.activation(probsT[:, HC * c:HC * (c + 1), :].rearrange("p h q -> p (h q)"),
                                     pT_bank[c % 2][:], ACT.Copy).then_inc(pT_ready, 1)

            def step(st):
                chunk = st.u % GB
                if st.has(-2):
                    wait(act, o_done, st, -2)
                    nc.scalar.activation(oT_hi[:].rearrange("p c q -> p (c q)"), bank_a[:],
                                         ACT.Copy).then_inc(o_hi_ready, 1)
                if st.has(-1):
                    if not st.has(3):
                        exps(st, -1, 2)
                    exps(st, -1, 3)
                if st.has(8):
                    if chunk == 0:
                        wait(act, v_done, st, 3)
                    wait(act, xT_done, st, 8)
                    nc.scalar.activation(xT_hi[st.group(8)][:, chunk, :], xT_raw[:],
                                         ACT.Copy).then_inc(xT_hi_ready, 1)
                if st.peeled and st.batch(0) == -GB - 1:
                    weight_hi(0)
                if st.peeled and st.batch(0) == -GB:
                    weight_hi(1)
                if st.has(4):
                    wait(act, q_done, st, 4)
                    nc.scalar.activation(qT[st.group(4)][:, chunk, :], bank_b[:], ACT.Identity,
                                         bias=bq_scaled[:, chunk:chunk + 1], scale=SCALE).then_inc(q_ready, 1)
                elif st.has(-1):
                    for c in range(KC):
                        probsT_out(st, c)
                if st.peeled and st.batch(0) == -GB:
                    weight_hi(2)
                    weight_hi(3)
                if st.has(0):
                    exps(st, 0, 0)
                if st.has(-1) and st.has(4):
                    probsT_out(st, 0)
                    probsT_out(st, 1)
                if st.has(0):
                    exps(st, 0, 1)
                if st.has(4):
                    wait(act, k_done, st, 4)
                    nc.scalar.activation(kT[st.group(4)][:, chunk, :], bank_a[:], ACT.Identity,
                                         bias=bk_col[:, chunk:chunk + 1]).then_inc(k_ready, 1)
                if st.has(-1) and st.has(4):
                    probsT_out(st, 2)
                    probsT_out(st, 3)
                if st.has(0) and st.has(4):
                    exps(st, 0, 2)

            run(act, step)

        @block.vector
        def _(dve):
            staging = [probs[0], probs[1], probsT, rows]
            dve.wait_ge(consts_loaded, 64)
            nc.vector.tensor_scalar(bq_scaled[:], bq_col[:], SCALE, None, ALU.mult).then_inc(bq_ready, 1)

            def weight_lo(w):
                dve.wait_ge(w_hi_ready, w + 1)
                nc.vector.tensor_tensor(w_lo[w][:].rearrange("p c n -> p (c n)"),
                                        staging[w][:].rearrange("p a b -> p (a b)"),
                                        w_hi[w][:].bitcast(F32).rearrange("p c n -> p (c n)"),
                                        ALU.subtract).then_inc(w_lo_ready, 1)

            def maxima(st, c):
                two = st.slot(0, 2)
                nc.vector.tensor_reduce(neg_max[:, two, HC * c:HC * (c + 1)],
                                        probs[two][:, HC * c:HC * (c + 1), :], axis=AX_X, op=ALU.max,
                                        negate=True).then_inc(max_ready, 1)

            def normalise(st, ahead, c):
                two = st.slot(ahead, 2)
                heads = slice(HC * c, HC * (c + 1))
                wait(dve, exp_ready, st, ahead, per=4, more=c + 1)
                nc.vector.reciprocal(inv_sum[:, two, heads], exp_sum[:, two, heads]).then_inc(inv_ready, 1)
                wait(dve, inv_ready, st, ahead, per=4, more=c + 1)
                nc.vector.tensor_tensor(probs[two][:, heads, :], probs[two][:, heads, :],
                                        inv_sum[:, two, heads].unsqueeze(2).broadcast_to([P, HC, S]),
                                        ALU.mult).then_inc(probs_ready, 1)

            def step(st):
                chunk, two = st.u % GB, st.slot(0, 2)
                slot, half = st.slot(-2, 4), st.slot(-2, 2)
                if st.has(-2):
                    wait(dve, o_hi_ready, st, -2)
                    nc.vector.tensor_tensor(oT_lo[:].rearrange("p c q -> p (c q)"), bank_a[:],
                                            oT_hi[:].bitcast(F32).rearrange("p c q -> p (c q)"),
                                            ALU.subtract).then_inc(o_lo_ready, 1)
                if st.has(-1):
                    normalise(st, -1, 2)
                    normalise(st, -1, 3)
                if st.has(8):
                    dve.wait_ge(x_loaded[chunk], 16 * HC * st.fills(8, GB))
                    wait(dve, xT_lo_ready, st, 7)
                    nc.vector.transpose(xT_raw[:], x_in[:, chunk, :]).then_inc(xT_done, 1)
                if st.has(-2):
                    wait(dve, y_done, st, -2)
                    wait(dve, bo_added, st, -2)
                    nc.vector.tensor_tensor(rows[:, slot, :], bank_b[:], rows[:, slot, :],
                                            ALU.add).then_inc(y_added, 1)
                    wait(dve, y_added, st, -2)
                    nc.vector.bn_stats(moments[:, half, :], rows[:, slot, :]).then_inc(moments_ready, 1)
                if st.has(0):
                    wait(dve, scores_done, st, 0)
                    wait(dve, mask_ready, st, 0)
                    if st.has(-2):
                        wait(dve, moments_ready, st, -2)
                    nc.vector.tensor_tensor(
                        probs[two][:].rearrange("p (c j) k -> p j c k", j=HC),
                        scores[:].rearrange("p j (c k) -> p j c k", c=KC),
                        mask_add[:, two, :].unsqueeze(1).unsqueeze(1).broadcast_to([P, HC, KC, S]),
                        ALU.add).then_inc(masked, 1)
                elif st.has(-2):
                    wait(dve, moments_ready, st, -2)
                if st.has(-2):
                    nc.vector.bn_aggr(mean_var[:, half, :], moments[:, half, :]).then_inc(mean_ready, 1)
                if st.has(8):
                    wait(dve, xT_hi_ready, st, 8)
                    nc.vector.tensor_tensor(xT_lo[st.group(8)][:, chunk, :], xT_raw[:],
                                            xT_hi[st.group(8)][:, chunk, :].bitcast(F32),
                                            ALU.subtract).then_inc(xT_lo_ready, 1)
                if st.peeled and st.batch(0) == -GB - 1:
                    weight_lo(0)
                if st.peeled and st.batch(0) == -GB:
                    for w in range(1, 4):
                        weight_lo(w)
                if st.has(0):
                    wait(dve, masked, st, 0)
                    for c in range(KC):
                        maxima(st, c)
                if st.has(-2):
                    wait(dve, rstd_ready, st, -2)
                    nc.vector.tensor_scalar(rows[:, slot, :], rows[:, slot, :], mean_var[:, half, 0:1],
                                            rstd[:, half:half + 1], ALU.subtract, ALU.mult).then_inc(normed, 1)
                if st.has(0):
                    normalise(st, 0, 0)
                    normalise(st, 0, 1)
                if st.has(4):
                    wait(dve, v_done, st, 4)
                    nc.vector.tensor_tensor(v[:, st.slot(4, ROUND), :], bank_b[:], bv_all[:],
                                            ALU.add).then_inc(v_ready, 1)

            run(dve, step)

        @block.tensor
        def _(pe):
            pe.wait_ge(ident_ready, 1)

            def three_passes(dst, left, right):
                for c in range(KC):
                    for a, b in ((0, 0), (0, 1), (1, 0)):
                        last = nc.tensor.matmul(dst, left[a](c), right[b](c), start=(c == 0 and a == b),
                                                stop=(c == KC - 1 and a == 1))
                return last

            def scores_of(st, chunks):
                cols = slice(st.u % GB * P, (st.u % GB + 1) * P)
                for c in chunks:
                    for j in range(HC):
                        rows_j = slice(DH * j, DH * (j + 1))
                        last = nc.tensor.matmul(scores[:, j, c * S:(c + 1) * S],
                                                qT[st.group(0)][rows_j, c, cols],
                                                kT[st.group(0)][rows_j, c, cols],
                                                start=True, stop=True, tile_position=(DH * j, 0))
                return last

            def probs_transposed(st, c):
                two = st.slot(-1, 2)
                wait(pe, probs_ready, st, -1, per=4, more=c + 1)
                wait(pe, pT_ready, st, -1, per=4, more=c - 1)
                for j in range(HC):
                    last = nc.tensor.transpose(pT_bank[c % 2][:, j * S:(j + 1) * S],
                                               probs[two][:, HC * c + j, :], ident[:])
                last.then_inc(pT_done, 1)

            def step(st):
                chunk = st.u % GB
                cols = slice(chunk * P, (chunk + 1) * P)
                g = st.group(4)
                if st.has(0):
                    if chunk == 0:
                        wait(pe, q_ready, st, 3)
                        wait(pe, k_ready, st, 3)
                    wait(pe, masked, st, -1)
                    scores_of(st, (0, 1))
                if st.has(-2):
                    if st.peeled and st.batch(-2) == 0:
                        pe.wait_ge(w_lo_ready, 4)
                    wait(pe, o_lo_ready, st, -2)
                    wait(pe, v_ready, st, 3)
                    wait(pe, y_added, st, -3)
                    three_passes(bank_b[:], [lambda c: oT_hi[:, c, :], lambda c: oT_lo[:, c, :]],
                                 [lambda c: w_hi[3][:, c, :], lambda c: w_lo[3][:, c, :]]).then_inc(y_done, 1)
                if st.has(0):
                    scores_of(st, (2, 3)).then_inc(scores_done, 1)
                if st.has(4):
                    if chunk == 0:
                        wait(pe, xT_lo_ready, st, 7)
                    if st.peeled and st.batch(4) == 0:
                        pe.wait_ge(w_lo_ready, 1)
                    wait(pe, y_added, st, -2)
                    wait(pe, v_ready, st, 3)
                    three_passes(bank_b[:], [lambda c: w_hi[0][:, c, cols], lambda c: w_lo[0][:, c, cols]],
                                 [lambda c: xT_hi[g][:, c, :], lambda c: xT_lo[g][:, c, :]]).then_inc(q_done, 1)
                if st.has(-1):
                    probs_transposed(st, 0)
                    probs_transposed(st, 1)
                if st.has(4):
                    if st.has(-2):
                        wait(pe, o_lo_ready, st, -2)
                    else:
                        wait(pe, k_ready, st, 3)
                    if st.peeled and st.batch(4) == 0:
                        pe.wait_ge(w_lo_ready, 2)
                    three_passes(bank_a[:], [lambda c: w_hi[1][:, c, cols], lambda c: w_lo[1][:, c, cols]],
                                 [lambda c: xT_hi[g][:, c, :], lambda c: xT_lo[g][:, c, :]]).then_inc(k_done, 1)
                if st.has(-1):
                    probs_transposed(st, 2)
                    probs_transposed(st, 3)
                if st.has(4):
                    wait(pe, q_ready, st, 4)
                    if st.peeled and st.batch(4) == 0:
                        pe.wait_ge(w_lo_ready, 3)
                    three_passes(bank_b[:], [lambda c: xT_hi[g][:, c, cols], lambda c: xT_lo[g][:, c, cols]],
                                 [lambda c: w_hi[2][:, c, :], lambda c: w_lo[2][:, c, :]]).then_inc(v_done, 1)
                if st.has(-1):
                    wait(pe, k_ready, st, 4)
                    wait(pe, v_ready, st, -1)
                    for c in range(KC):
                        wait(pe, pT_ready, st, -1, per=4, more=c + 1)
                        for j in range(HC):
                            h = HC * c + j
                            last = nc.tensor.matmul(bank_a[DH * j:DH * (j + 1), c * S:(c + 1) * S],
                                                    v[:, st.slot(-1, ROUND), DH * h:DH * (h + 1)],
                                                    probsT[:, h, :], start=True, stop=True,
                                                    tile_position=(0, DH * j))
                    last.then_inc(o_done, 1)

            run(pe, step)


_INS = ['x', 'adj', 'L0_gnn_Wq', 'L0_gnn_bq', 'L0_gnn_Wk', 'L0_gnn_bk', 'L0_gnn_Wv', 'L0_gnn_bv',
        'L0_gnn_Wo', 'L0_gnn_bo']


def kernel(**inputs):
    import numpy as _np
    import concourse.bacc as _bacc
    from concourse import mybir as _mybir
    from concourse.bass_utils import run_bass_kernel_spmd as _run

    nc = _bacc.Bacc("TRN2", target_bir_lowering=False, num_devices=1)
    arrays, args = {}, []
    for name in _INS:
        a = _np.ascontiguousarray(inputs[name])
        arrays[f"in_{name}_dram"] = a
        args.append(nc.dram_tensor(f"in_{name}_dram", a.shape, _mybir.dt.from_np(a.dtype), kind="ExternalInput").ap())
    shape = arrays["in_x_dram"].shape
    args.append(nc.dram_tensor("out_dram", shape, _mybir.dt.float32, kind="ExternalOutput").ap())
    gnn_attention(nc, *args)
    r = _run(nc, [arrays], core_ids=[0])
    return r.results[0]["out_dram"]
```

```python
from contextlib import ExitStack

import concourse.bass as bass
from concourse import mybir

ALU = mybir.AluOpType
ACT = mybir.ActivationFunctionType
F32 = mybir.dt.float32
F32R = mybir.dt.float32r
I32 = mybir.dt.int32
AX_X = mybir.AxisListType.X

P = 128
GB = 4
ROUND = 8
DH = 32
MASKED = -3.0e38
EPS = 1e-5


def gnn_attention(nc, x, adj, Wq, bq, Wk, bk, Wv, bv, Wo, bo, out):
    NB, S, D = x.shape
    KC = D // P
    H = D // DH
    HC = H // KC
    TOK = GB * S
    SCALE = float(DH) ** -0.5
    assert S == P and KC == GB == HC == 4 and NB % ROUND == 0

    FIRST, LAST = -ROUND, NB + 1
    BODY = 3
    ROUNDS = (NB - ROUND - BODY) // ROUND
    TAIL = BODY + ROUND * ROUNDS

    with ExitStack() as ctx:

        def sb(name, shape, dt=F32):
            return ctx.enter_context(nc.sbuf_tensor(name, shape, dt))

        def bank(name, shape):
            return ctx.enter_context(nc.psum_tensor(name, shape, F32))

        def sem(name):
            return ctx.enter_context(nc.semaphore(name))

        w_hi = [sb(f"w{w}_hi", [P, KC, D], F32R) for w in "kqvo"]
        w_lo = [sb(f"w{w}_lo", [P, KC, D], F32R) for w in "kqvo"]
        x_in = sb("x_in", [P, 2, TOK])
        xT_raw = sb("xT_raw", [P, TOK])
        xT_hi = [sb(f"xT_hi{i}", [P, KC, TOK], F32R) for i in range(2)]
        xT_lo = [sb(f"xT_lo{i}", [P, KC, TOK], F32R) for i in range(2)]
        qT = [sb(f"qT{i}", [P, KC, TOK]) for i in range(2)]
        q_hi = sb("q_hi", [P, KC, S], F32R)
        q_lo = sb("q_lo", [P, KC, S], F32R)
        k_blocks_hi = sb("k_blocks_hi", [P, KC, HC * S], F32R)
        k_blocks_lo = sb("k_blocks_lo", [P, KC, HC * S], F32R)
        kT = [sb(f"kT{i}", [P, KC, TOK]) for i in range(2)]
        v = sb("v", [P, ROUND, D])
        probs = [sb(f"probs{i}", [P, H, S]) for i in range(2)]
        probsT = sb("probsT", [P, 2 * HC, S])
        oT_hi = sb("oT_hi", [P, KC, S], F32R)
        oT_lo = sb("oT_lo", [P, KC, S], F32R)
        rows = sb("rows", [P, 2, D])
        adj_in = sb("adj_in", [P, 4, S], I32)
        mask_add = sb("mask_add", [P, 2, S])
        ident = sb("ident", [P, P])
        bq_col = sb("bq_col", [P, KC])
        bq_scaled = sb("bq_scaled", [P, KC])
        bk_col = sb("bk_col", [P, KC])
        bv_all = sb("bv_all", [P, D])
        bo_all = sb("bo_all", [P, D])
        neg_max = sb("neg_max", [P, 2, H])
        exp_sum = sb("exp_sum", [P, 2, H])
        inv_sum = sb("inv_sum", [P, 2, H])
        moments = sb("moments", [P, 2, 6])
        mean_var = sb("mean_var", [P, 2, 2])
        var_eps = sb("var_eps", [P, 2])
        rstd = sb("rstd", [P, 2])
        minus_half = sb("minus_half", [P, 1])
        eps = sb("eps", [P, 1])

        scores = bank("scores", [P, KC, HC * S])
        pT_bank = [bank(f"pT_bank{i}", [P, HC * S]) for i in range(2)]
        bank_a = bank("bank_a", [P, D])
        bank_b = bank("bank_b", [P, D])

        w_loaded = [[sem(f"w{w}_loaded{i}") for i in range(KC)] for w in "kqvo"]
        bqk_loaded, bv_loaded, bo_loaded = sem("bqk_loaded"), sem("bv_loaded"), sem("bo_loaded")
        x_loaded = [sem(f"x_loaded{i}") for i in range(2)]
        x_first_loaded = [sem(f"x_first_loaded{i}") for i in range(2)]
        adj_loaded = [sem(f"adj_loaded{i}") for i in range(4)]
        rows_loaded = [sem(f"rows_loaded{i}") for i in range(2)]
        rows_stored = [sem(f"rows_stored{i}") for i in range(2)]
        cleared = sem("cleared")
        ident_ready = sem("ident_ready")
        w_hi_ready, w_lo_ready = sem("w_hi_ready"), sem("w_lo_ready")
        bq_ready = sem("bq_ready")
        xT_done, xT_hi_ready, xT_lo_ready = sem("xT_done"), sem("xT_hi_ready"), sem("xT_lo_ready")
        q_done, q_ready = sem("q_done"), sem("q_ready")
        k_done, k_ready = sem("k_done"), sem("k_ready")
        v_done, v_ready = sem("v_done"), sem("v_ready")
        q_hi_ready, q_lo_ready, mask_ready = sem("q_hi_ready"), sem("q_lo_ready"), sem("mask_ready")
        o_hi_ready, o_lo_ready = sem("o_hi_ready"), sem("o_lo_ready")
        y_done, y_added, bo_added = sem("y_done"), sem("y_added"), sem("bo_added")
        moments_ready, mean_ready = sem("moments_ready"), sem("mean_ready")
        var_ready, rstd_ready, normed = sem("var_ready"), sem("rstd_ready"), sem("normed")
        k_lo01_ready, k_lo23_ready = sem("k_lo01_ready"), sem("k_lo23_ready")
        k_hi_ready = sem("k_hi_ready")
        scores_done, masked = sem("scores_done"), sem("masked")
        max_ready, exp_ready = sem("max_ready"), sem("exp_ready")
        inv_ready, probs_ready = sem("inv_ready"), sem("probs_ready")
        pT_done, pT_ready, o_done = sem("pT_done"), sem("pT_ready"), sem("o_done")

        def w_staged(w, c):
            return probs[w][:, HC * c:HC * (c + 1), :].rearrange("p h k -> p (h k)") if w < 2 else v[:, GB * (w - 2) + c, :]

        class Step:

            def __init__(self, n, u):
                self.n, self.u = n, u
                self.peeled = isinstance(n, int)

            def has(self, ahead):
                return not self.peeled or 0 <= ROUND * self.n + self.u + ahead < NB

            def no_projections_left(self):
                return self.peeled and ROUND * self.n + self.u + GB >= NB

            def slot(self, ahead, slots):
                return (self.u + ahead) % slots

            def group(self, ahead):
                return (self.u + ahead) // GB % 2

            def tokens(self, ahead):
                return slice((self.u + ahead) % GB * P, ((self.u + ahead) % GB + 1) * P)

            def fills(self, ahead, slots):
                return (ROUND // slots) * self.n + (self.u + ahead) // slots + 1

            def batch(self, ahead):
                return ROUND * self.n + (self.u + ahead)

        def wait(eng, semaphore, step, ahead, per=1, more=0):
            if step.peeled:
                upto = per * step.batch(ahead) + (more if per > 1 else 1)
                upto = min(upto, per * NB)
                if upto > 0:
                    eng.wait_ge(semaphore, upto)
            else:
                eng.wait_ge(semaphore, per * ROUND * step.n + (per * (step.u + ahead) + (more if per > 1 else 1)))

        def k_low_operands(st, j):
            rows_j, keys_j = slice(DH * j, DH * (j + 1)), slice(j * S, (j + 1) * S)
            return (k_blocks_lo[rows_j, :, keys_j], kT[st.group(1)][rows_j, :, st.tokens(1)],
                    k_blocks_hi[rows_j, :, keys_j].bitcast(F32))

        def q_bank(st):
            return bank_a if st.has(-1) else bank_b

        def v_bank(st):
            return bank_a if st.has(-1) else pT_bank[0]

        def y_bank(st):
            return bank_a if st.no_projections_left() else bank_b

        def run(eng, do_step):
            for s in range(FIRST, BODY):
                do_step(Step(s // ROUND, s % ROUND))
            with eng.Fori(0, ROUNDS) as n:
                for u in range(BODY, BODY + ROUND):
                    do_step(Step(n, u))
            for s in range(TAIL, LAST + 1):
                do_step(Step(s // ROUND, s % ROUND))

        block = ctx.enter_context(nc.Block())

        @block.sync
        def _(sp):
            def load_x(batch, c, dst, loaded):
                blocks = x[bass.ds(batch, GB)].rearrange("b (k t) (c q f) -> c q t (b k) f", t=DH, q=HC, f=DH)
                for q in range(HC):
                    sp.dma_start(dst[DH * q:DH * (q + 1), :].rearrange("t (b f) -> t b f", f=DH),
                                 blocks[c, q]).then_inc(loaded, 16)

            def load_weight(w, dram, chunks=range(KC)):
                for c in chunks:
                    sp.dma_start(w_staged(w, c), dram[c * P:(c + 1) * P, :]).then_inc(w_loaded[w][c], 16)

            for c in range(KC):
                load_x(0, c, x_in[:, c, :] if c < 2 else rows[:, c - 2, :],
                       x_loaded[c] if c < 2 else x_first_loaded[c - 2])
                load_weight(0, Wk, [c])
            sp.dma_start(bk_col[:], bk.rearrange("(c p) -> p c", p=P),
                         allow_slow_non_contiguous=True).then_inc(bqk_loaded, 16)
            sp.dma_start(bq_col[:], bq.rearrange("(c p) -> p c", p=P),
                         allow_slow_non_contiguous=True).then_inc(bqk_loaded, 16)
            load_weight(1, Wq)

            def step(st):
                u = st.u
                if st.has(-1):
                    slot = st.slot(-1, 2)
                    if st.peeled and st.batch(-1) < 2:
                        wait(sp, xT_done, st, 3)
                    else:
                        sp.wait_ge(rows_stored[slot], 16 * (st.fills(-1, 2) - 1))
                    sp.dma_start(rows[:, slot, :],
                                 x[bass.ds(st.batch(-1), 1)].rearrange("b t d -> t (b d)")
                                 ).then_inc(rows_loaded[slot], 16)
                c = (u + 2) % KC
                if st.has(10 - c) and not (st.peeled and st.batch(0) < FIRST + 2):
                    wait(sp, xT_done, st, 8)
                    load_x(st.batch(10 - c), c, x_in[:, c % 2, :], x_loaded[c % 2])
                if st.peeled and st.batch(0) == FIRST + 2:
                    load_weight(2, Wv)
                    sp.dma_start(bv_all[:], bv.partition_broadcast(P)).then_inc(bv_loaded, 16)
                if st.peeled and st.batch(0) == FIRST + 3:
                    load_weight(3, Wo)
                    sp.dma_start(bo_all[:], bo.partition_broadcast(P)).then_inc(bo_loaded, 16)
                if st.has(4):
                    slot = st.slot(4, 4)
                    wait(sp, mask_ready, st, 0)
                    sp.dma_start(adj_in[:, slot, :], adj[bass.ds(st.batch(4), 1)].rearrange("b q k -> q (b k)")
                                 ).then_inc(adj_loaded[slot], 16)
                if st.has(-2):
                    slot = st.slot(-2, 2)
                    wait(sp, normed, st, -2)
                    sp.dma_start(out[bass.ds(st.batch(-2), 1)].rearrange("b t d -> t (b d)"),
                                 rows[:, slot, :]).then_inc(rows_stored[slot], 16)

            run(sp, step)
            for slot in range(2):
                sp.wait_ge(rows_stored[slot], 16 * (NB // 2))

        @block.gpsimd
        def _(pool):
            nc.gpsimd.memset(ident[:], 0.0).then_inc(cleared, 1)
            nc.gpsimd.memset(minus_half[:], -0.5).then_inc(cleared, 1)
            nc.gpsimd.memset(eps[:], EPS).then_inc(cleared, 1)
            pool.wait_ge(cleared, 3)
            nc.gpsimd.affine_select(out=ident[:], in_=ident[:], compare_op=ALU.not_equal, fill=1.0, base=0,
                                    pattern=[[-1, P]], channel_multiplier=1).then_inc(ident_ready, 1)
            nc.gpsimd.memset(k_blocks_hi[:].bitcast(F32), 0.0).then_inc(cleared, 1)
            nc.gpsimd.memset(k_blocks_lo[:].bitcast(F32), 0.0).then_inc(cleared, 1)
            pool.wait_ge(cleared, 5)

            def step(st):
                wait(pool, k_lo01_ready, st, 0, per=2, more=2)
                if st.has(1):
                    pool.wait_ge(adj_loaded[st.slot(1, 4)], 16 * st.fills(1, 4))
                    wait(pool, masked, st, -1, per=4, more=4)
                if st.has(-2):
                    slot = st.slot(-2, 2)
                    if st.peeled and st.batch(-2) == 0:
                        pool.wait_ge(bo_loaded, 16)
                    pool.wait_ge(rows_loaded[slot], 16 * st.fills(-2, 2))
                    nc.gpsimd.tensor_tensor(rows[:, slot, :], rows[:, slot, :], bo_all[:],
                                            ALU.add).then_inc(bo_added, 1)
                if st.has(1):
                    nc.gpsimd.tensor_scalar(mask_add[:, st.slot(1, 2), :],
                                            adj_in[:, st.slot(1, 4), :],
                                            0.0, MASKED, ALU.is_equal, ALU.mult).then_inc(mask_ready, 1)
                if st.has(1):
                    wait(pool, mask_ready, st, 1)
                    wait(pool, bo_added, st, -2)
                    for j in (0, 1):
                        wait(pool, k_lo01_ready, st, 1, per=2, more=j)
                        wait(pool, k_hi_ready, st, 1, per=4, more=j + 1)
                        nc.gpsimd.tensor_tensor(*k_low_operands(st, j), ALU.subtract).then_inc(k_lo01_ready, 1)
                if st.has(-2):
                    two = st.slot(-2, 2)
                    wait(pool, k_lo01_ready, st, 1, per=2, more=2)
                    wait(pool, mean_ready, st, -2)
                    nc.gpsimd.tensor_tensor(var_eps[:, two:two + 1], mean_var[:, two, 1:2], eps[:],
                                            ALU.add).then_inc(var_ready, 1)
                    wait(pool, var_ready, st, -2)
                    nc.gpsimd.tensor_tensor(rstd[:, two:two + 1], var_eps[:, two:two + 1], minus_half[:],
                                            ALU.pow).then_inc(rstd_ready, 1)

            run(pool, step)

        @block.scalar
        def _(act):
            def weight_hi(w, chunks=range(KC)):
                for c in chunks:
                    act.wait_ge(w_loaded[w][c], 16)
                    nc.scalar.activation(w_hi[w][:, c, :], w_staged(w, c), ACT.Copy).then_inc(w_hi_ready, 1)

            def exps(st, ahead, c):
                two = st.slot(ahead, 2)
                wait(act, max_ready, st, ahead, per=4, more=c + 1)
                for h in range(HC * c, HC * (c + 1)):
                    last = nc.scalar.activation(probs[two][:, h, :], probs[two][:, h, :], ACT.Exp,
                                                bias=neg_max[:, two, h:h + 1],
                                                accum_out=exp_sum[:, two, h:h + 1])
                last.then_inc(exp_ready, 1)

            def k_high(st, heads):
                for j in heads:
                    rows_j = slice(DH * j, DH * (j + 1))
                    nc.scalar.activation(k_blocks_hi[rows_j, :, j * S:(j + 1) * S],
                                         kT[st.group(1)][rows_j, :, st.tokens(1)],
                                         ACT.Copy).then_inc(k_hi_ready, 1)

            def oT_high(st):
                wait(act, o_done, st, -2, per=4, more=4)
                nc.scalar.activation(oT_hi[:].rearrange("p c q -> p (c q)"), bank_b[:],
                                     ACT.Copy).then_inc(o_hi_ready, 1)

            def q_high(st):
                nc.scalar.activation(q_hi[:], qT[st.group(1)][:, :, st.tokens(1)],
                                     ACT.Copy).then_inc(q_hi_ready, 1)

            def probsT_out(st, c):
                wait(act, pT_done, st, -1, per=4, more=c + 1)
                if c >= 2:
                    wait(act, o_done, st, -1, per=4, more=c - 1)
                nc.scalar.activation(probsT[:, c % 2 * HC:(c % 2 + 1) * HC, :].rearrange("p h q -> p (h q)"),
                                     pT_bank[c % 2][:], ACT.Copy).then_inc(pT_ready, 1)

            def last_step(st):
                if st.has(-2):
                    oT_high(st)
                if st.has(-1):
                    exps(st, -1, 3)
                if st.has(1):
                    wait(act, scores_done, st, 0, per=4, more=4)
                    k_high(st, range(HC))
                    q_high(st)
                if st.has(-1):
                    probsT_out(st, 0)
                    probsT_out(st, 1)
                if st.has(0):
                    exps(st, 0, 0)
                if st.has(-1):
                    probsT_out(st, 2)
                    probsT_out(st, 3)
                if st.has(0):
                    exps(st, 0, 1)
                    exps(st, 0, 2)

            def step(st):
                if st.no_projections_left():
                    last_step(st)
                    return
                chunk = st.u % GB
                if st.has(-2):
                    oT_high(st)
                if st.has(-1):
                    probsT_out(st, 0)
                    probsT_out(st, 1)
                    exps(st, -1, 3)
                if st.peeled and st.batch(0) < -GB:
                    weight_hi(0, [chunk])
                if st.has(8):
                    if chunk == 0:
                        wait(act, v_done, st, 3)
                    wait(act, xT_done, st, 8)
                    nc.scalar.activation(xT_hi[st.group(8)][:, chunk, :], xT_raw[:],
                                         ACT.Copy).then_inc(xT_hi_ready, 1)
                if st.peeled and st.batch(0) == -GB - 1:
                    weight_hi(1)
                if st.peeled and st.batch(0) == -GB:
                    act.wait_ge(bqk_loaded, 32)
                    act.wait_ge(bq_ready, 1)
                if st.has(0):
                    exps(st, 0, 0)
                if st.has(4):
                    wait(act, k_done, st, 4)
                    nc.scalar.activation(kT[st.group(4)][:, chunk, :], bank_a[:], ACT.Identity,
                                         bias=bk_col[:, chunk:chunk + 1]).then_inc(k_ready, 1)
                if st.peeled and st.batch(0) == -GB:
                    weight_hi(2)
                if st.peeled and st.batch(0) == -GB + 1:
                    weight_hi(3)
                if st.has(1):
                    if st.peeled and st.batch(0) == -1:
                        act.wait_ge(cleared, 5)
                    wait(act, k_ready, st, 4)
                    wait(act, scores_done, st, 0, per=4, more=4)
                    k_high(st, (0, 1))
                if st.has(0):
                    exps(st, 0, 1)
                if st.has(1):
                    k_high(st, (2, 3))
                if st.has(4):
                    wait(act, q_done, st, 4)
                    nc.scalar.activation(qT[st.group(4)][:, chunk, :], q_bank(st)[:], ACT.Identity,
                                         bias=bq_scaled[:, chunk:chunk + 1], scale=SCALE).then_inc(q_ready, 1)
                if st.has(1):
                    wait(act, q_ready, st, 4)
                    q_high(st)
                if st.has(-1):
                    probsT_out(st, 2)
                    probsT_out(st, 3)
                if st.has(0):
                    exps(st, 0, 2)

            run(act, step)

        @block.vector
        def _(dve):
            def weight_lo(w, chunks=range(KC)):
                for c in chunks:
                    dve.wait_ge(w_hi_ready, KC * w + c + 1)
                    nc.vector.tensor_tensor(w_lo[w][:, c, :], w_staged(w, c), w_hi[w][:, c, :].bitcast(F32),
                                            ALU.subtract).then_inc(w_lo_ready, 1)

            def masked_scores(st, c):
                two = st.slot(0, 2)
                wait(dve, scores_done, st, 0, per=4, more=c + 1)
                nc.vector.tensor_tensor(probs[two][:, HC * c:HC * (c + 1), :],
                                        scores[:, c, :].rearrange("p (j k) -> p j k", j=HC),
                                        mask_add[:, two, :].unsqueeze(1).broadcast_to([P, HC, S]),
                                        ALU.add).then_inc(masked, 1)

            def maxima(st, c):
                two = st.slot(0, 2)
                wait(dve, masked, st, 0, per=4, more=c + 1)
                nc.vector.tensor_reduce(neg_max[:, two, HC * c:HC * (c + 1)],
                                        probs[two][:, HC * c:HC * (c + 1), :], axis=AX_X, op=ALU.max,
                                        negate=True).then_inc(max_ready, 1)

            def normalise(st, ahead, c):
                two = st.slot(ahead, 2)
                heads = slice(HC * c, HC * (c + 1))
                wait(dve, exp_ready, st, ahead, per=4, more=c + 1)
                nc.vector.reciprocal(inv_sum[:, two, heads], exp_sum[:, two, heads]).then_inc(inv_ready, 1)
                wait(dve, inv_ready, st, ahead, per=4, more=c + 1)
                nc.vector.tensor_tensor(probs[two][:, heads, :], probs[two][:, heads, :],
                                        inv_sum[:, two, heads].unsqueeze(2).broadcast_to([P, HC, S]),
                                        ALU.mult).then_inc(probs_ready, 1)

            def oT_low(st):
                wait(dve, o_hi_ready, st, -2)
                nc.vector.tensor_tensor(oT_lo[:].rearrange("p c q -> p (c q)"), bank_b[:],
                                        oT_hi[:].bitcast(F32).rearrange("p c q -> p (c q)"),
                                        ALU.subtract).then_inc(o_lo_ready, 1)

            def x_transposed(st):
                chunk = st.u % GB
                src = x_in[:, chunk % 2, :]
                if st.peeled and st.batch(8) in (2, 3):
                    src = rows[:, chunk - 2, :]
                    dve.wait_ge(x_first_loaded[chunk - 2], 16 * HC)
                elif st.peeled and st.batch(8) < 2:
                    dve.wait_ge(x_loaded[chunk], 16 * HC)
                else:
                    dve.wait_ge(x_loaded[chunk % 2], 16 * HC * (st.fills(8, 2) - 1))
                wait(dve, xT_lo_ready, st, 7)
                nc.vector.transpose(xT_raw[:], src).then_inc(xT_done, 1)

            def y_and_moments(st):
                two = st.slot(-2, 2)
                wait(dve, y_done, st, -2)
                wait(dve, bo_added, st, -2)
                nc.vector.tensor_tensor(rows[:, two, :], y_bank(st)[:], rows[:, two, :],
                                        ALU.add).then_inc(y_added, 1)
                wait(dve, y_added, st, -2)
                nc.vector.bn_stats(moments[:, two, :], rows[:, two, :]).then_inc(moments_ready, 1)

            def mean_and_variance(st):
                two = st.slot(-2, 2)
                nc.vector.bn_aggr(mean_var[:, two, :], moments[:, two, :]).then_inc(mean_ready, 1)

            def result(st):
                two = st.slot(-2, 2)
                wait(dve, rstd_ready, st, -2)
                nc.vector.tensor_scalar(rows[:, two, :], rows[:, two, :], mean_var[:, two, 0:1],
                                        rstd[:, two:two + 1], ALU.subtract, ALU.mult).then_inc(normed, 1)

            def k_low(st):
                for j in (2, 3):
                    wait(dve, k_hi_ready, st, 1, per=4, more=j + 1)
                    nc.vector.tensor_tensor(*k_low_operands(st, j), ALU.subtract).then_inc(k_lo23_ready, 1)

            def q_low(st):
                wait(dve, q_hi_ready, st, 1)
                nc.vector.tensor_tensor(q_lo[:], qT[st.group(1)][:, :, st.tokens(1)], q_hi[:].bitcast(F32),
                                        ALU.subtract).then_inc(q_lo_ready, 1)

            def last_step(st):
                if st.has(-2):
                    oT_low(st)
                if st.has(-1):
                    normalise(st, -1, 2)
                if st.has(0):
                    wait(dve, mask_ready, st, 0)
                    masked_scores(st, 0)
                    masked_scores(st, 1)
                    maxima(st, 0)
                    maxima(st, 1)
                    masked_scores(st, 2)
                    masked_scores(st, 3)
                if st.has(-1):
                    normalise(st, -1, 3)
                if st.has(1):
                    k_low(st)
                    q_low(st)
                if st.has(0):
                    maxima(st, 2)
                if st.has(-2):
                    y_and_moments(st)
                    wait(dve, moments_ready, st, -2)
                if st.has(0):
                    maxima(st, 3)
                if st.has(-2):
                    mean_and_variance(st)
                if st.has(0):
                    normalise(st, 0, 0)
                    normalise(st, 0, 1)
                if st.has(-2):
                    result(st)

            def step(st):
                if st.no_projections_left():
                    last_step(st)
                    return
                chunk = st.u % GB
                if st.has(-2):
                    oT_low(st)
                if st.has(8):
                    x_transposed(st)
                if st.peeled and st.batch(0) < -GB:
                    weight_lo(0, [chunk])
                if st.has(0):
                    wait(dve, mask_ready, st, 0)
                    masked_scores(st, 0)
                    masked_scores(st, 1)
                    maxima(st, 0)
                    maxima(st, 1)
                    masked_scores(st, 2)
                    masked_scores(st, 3)
                if st.has(-1):
                    normalise(st, -1, 2)
                    normalise(st, -1, 3)
                if st.has(0):
                    maxima(st, 2)
                if st.has(-2):
                    y_and_moments(st)
                    wait(dve, moments_ready, st, -2)
                if st.has(0):
                    maxima(st, 3)
                if st.has(-2):
                    mean_and_variance(st)
                if st.has(8):
                    wait(dve, xT_hi_ready, st, 8)
                    nc.vector.tensor_tensor(xT_lo[st.group(8)][:, chunk, :], xT_raw[:],
                                            xT_hi[st.group(8)][:, chunk, :].bitcast(F32),
                                            ALU.subtract).then_inc(xT_lo_ready, 1)
                if st.has(1):
                    k_low(st)
                if st.peeled and st.batch(0) == -GB - 1:
                    dve.wait_ge(bqk_loaded, 32)
                    nc.vector.tensor_scalar(bq_scaled[:], bq_col[:], SCALE, None, ALU.mult).then_inc(bq_ready, 1)
                    weight_lo(1)
                if st.peeled and st.batch(0) == -GB:
                    weight_lo(2)
                    dve.wait_ge(bv_loaded, 16)
                if st.peeled and st.batch(0) == -GB + 1:
                    weight_lo(3)
                if st.has(1) and not st.has(-1):
                    q_low(st)
                if st.has(0):
                    normalise(st, 0, 0)
                    normalise(st, 0, 1)
                if st.has(-2):
                    result(st)
                if st.has(1) and st.has(-1):
                    q_low(st)
                if st.has(4):
                    wait(dve, v_done, st, 4)
                    nc.vector.tensor_tensor(v[:, st.slot(4, ROUND), :], v_bank(st)[:], bv_all[:],
                                            ALU.add).then_inc(v_ready, 1)

            run(dve, step)

        @block.tensor
        def _(pe):
            pe.wait_ge(ident_ready, 1)

            def three_passes(dst, left, right, first_use_of=None):
                for c in range(KC):
                    if first_use_of is not None:
                        pe.wait_ge(w_lo_ready, KC * first_use_of + c + 1)
                        pe.wait_ge(xT_lo_ready, c + 1)
                    for a, b in ((0, 0), (0, 1), (1, 0)):
                        last = nc.tensor.matmul(dst, left[a](c), right[b](c), start=(c == 0 and a == b),
                                                stop=(c == KC - 1 and a == 1))
                return last

            def scores_of(st, c):
                wait(pe, masked, st, -1, per=4, more=c + 1)
                nc.tensor.matmul(scores[:, c, :], q_hi[:, c, :], k_blocks_hi[:, c, :], start=True, stop=False)
                nc.tensor.matmul(scores[:, c, :], q_hi[:, c, :], k_blocks_lo[:, c, :], start=False, stop=False)
                nc.tensor.matmul(scores[:, c, :], q_lo[:, c, :], k_blocks_hi[:, c, :], start=False,
                                 stop=True).then_inc(scores_done, 1)

            def probs_transposed(st, c):
                two = st.slot(-1, 2)
                wait(pe, probs_ready, st, -1, per=4, more=c + 1)
                wait(pe, pT_ready, st, -1, per=4, more=c - 1)
                for j in range(HC):
                    last = nc.tensor.transpose(pT_bank[c % 2][:, j * S:(j + 1) * S],
                                               probs[two][:, HC * c + j, :], ident[:])
                last.then_inc(pT_done, 1)

            def attention_out(st, c):
                wait(pe, pT_ready, st, -1, per=4, more=c + 1)
                for j in range(HC):
                    h = HC * c + j
                    last = nc.tensor.matmul(bank_b[DH * j:DH * (j + 1), c * S:(c + 1) * S],
                                            v[:, st.slot(-1, ROUND), DH * h:DH * (h + 1)],
                                            probsT[:, c % 2 * HC + j, :], start=True, stop=True,
                                            tile_position=(0, DH * j))
                last.then_inc(o_done, 1)

            def scores_all(st):
                wait(pe, k_lo01_ready, st, 0, per=2, more=2)
                wait(pe, k_lo23_ready, st, 0, per=2, more=2)
                wait(pe, q_lo_ready, st, 0)
                for c in range(KC):
                    scores_of(st, c)

            def output_projection(st):
                if st.peeled and st.batch(-2) == 0:
                    pe.wait_ge(w_lo_ready, KC * 4)
                wait(pe, o_lo_ready, st, -2)
                if st.no_projections_left():
                    wait(pe, v_ready, st, 3)
                    wait(pe, y_added, st, -3)
                three_passes(y_bank(st)[:], [lambda c: oT_hi[:, c, :], lambda c: oT_lo[:, c, :]],
                             [lambda c: w_hi[3][:, c, :], lambda c: w_lo[3][:, c, :]]).then_inc(y_done, 1)

            def last_step(st):
                if st.has(0):
                    scores_all(st)
                if st.has(-1):
                    probs_transposed(st, 0)
                    probs_transposed(st, 1)
                if st.has(-2):
                    output_projection(st)
                if st.has(-1):
                    wait(pe, o_lo_ready, st, -2)
                    wait(pe, y_added, st, -3)
                    attention_out(st, 0)
                    attention_out(st, 1)
                    probs_transposed(st, 2)
                    probs_transposed(st, 3)
                    attention_out(st, 2)
                    attention_out(st, 3)

            def step(st):
                if st.no_projections_left():
                    last_step(st)
                    return
                chunk = st.u % GB
                cols = st.tokens(0)
                first = st.peeled and st.batch(4) == 0
                g = st.group(4)
                first_probs = st.peeled and st.batch(-1) == 0
                if st.has(-1) and not first_probs:
                    probs_transposed(st, 0)
                    probs_transposed(st, 1)
                if st.has(0):
                    scores_all(st)
                if first_probs:
                    wait(pe, v_ready, st, 3)
                    probs_transposed(st, 0)
                    probs_transposed(st, 1)
                if st.has(4):
                    if chunk == 0 and not first:
                        wait(pe, xT_lo_ready, st, 7)
                    if st.has(-2):
                        wait(pe, v_ready, st, 3)
                    else:
                        wait(pe, k_ready, st, 3)
                    three_passes(bank_a[:], [lambda c: w_hi[0][:, c, cols], lambda c: w_lo[0][:, c, cols]],
                                 [lambda c: xT_hi[g][:, c, :], lambda c: xT_lo[g][:, c, :]],
                                 first_use_of=0 if first else None).then_inc(k_done, 1)
                if st.has(-2):
                    output_projection(st)
                if st.has(4):
                    if st.has(-1):
                        wait(pe, k_ready, st, 4)
                    else:
                        wait(pe, q_ready, st, 3)
                    three_passes(q_bank(st)[:], [lambda c: w_hi[1][:, c, cols], lambda c: w_lo[1][:, c, cols]],
                                 [lambda c: xT_hi[g][:, c, :], lambda c: xT_lo[g][:, c, :]],
                                 first_use_of=1 if first else None).then_inc(q_done, 1)
                if st.has(-1):
                    if st.has(-2):
                        wait(pe, y_added, st, -2)
                    else:
                        wait(pe, q_ready, st, 3)
                    wait(pe, v_ready, st, -1)
                    attention_out(st, 0)
                    attention_out(st, 1)
                    probs_transposed(st, 2)
                    probs_transposed(st, 3)
                if st.has(4):
                    if st.has(-1):
                        wait(pe, q_ready, st, 4)
                    else:
                        wait(pe, v_ready, st, 3)
                    three_passes(v_bank(st)[:], [lambda c: xT_hi[g][:, c, cols], lambda c: xT_lo[g][:, c, cols]],
                                 [lambda c: w_hi[2][:, c, :], lambda c: w_lo[2][:, c, :]],
                                 first_use_of=2 if first else None).then_inc(v_done, 1)
                if st.has(-1):
                    attention_out(st, 2)
                    attention_out(st, 3)

            run(pe, step)


_INS = ['x', 'adj', 'L0_gnn_Wq', 'L0_gnn_bq', 'L0_gnn_Wk', 'L0_gnn_bk', 'L0_gnn_Wv', 'L0_gnn_bv',
        'L0_gnn_Wo', 'L0_gnn_bo']


def kernel(**inputs):
    import numpy as _np
    import concourse.bacc as _bacc
    from concourse import mybir as _mybir
    from concourse.bass_utils import run_bass_kernel_spmd as _run

    nc = _bacc.Bacc("TRN2", target_bir_lowering=False, num_devices=1)
    arrays, args = {}, []
    for name in _INS:
        a = _np.ascontiguousarray(inputs[name])
        arrays[f"in_{name}_dram"] = a
        args.append(nc.dram_tensor(f"in_{name}_dram", a.shape, _mybir.dt.from_np(a.dtype), kind="ExternalInput").ap())
    shape = arrays["in_x_dram"].shape
    args.append(nc.dram_tensor("out_dram", shape, _mybir.dt.float32, kind="ExternalOutput").ap())
    gnn_attention(nc, *args)
    r = _run(nc, [arrays], core_ids=[0])
    return r.results[0]["out_dram"]
```
